# Optimizing a Trainium2 kernel written in Bass

```python
import numpy as np
import jax
import jax.numpy as jnp

def _softmax(x, axis=-1):
    return jax.nn.softmax(x, axis=axis)

def _gelu(x):
    return jax.nn.gelu(x, approximate=True)

def _silu(x):
    return jax.nn.silu(x)

def _sigmoid(x):
    return jax.nn.sigmoid(x)

def _layernorm(x, axis=-1, eps=1e-05):
    m = jnp.mean(x, axis=axis, keepdims=True)
    v = jnp.var(x, axis=axis, keepdims=True)
    return (x - m) / jnp.sqrt(v + eps)

def _scatter_add(tgt, idx, src, axis=0):
    return tgt.at[idx].add(src)

def _segment_sum(src, seg, n):
    return jax.ops.segment_sum(src, seg, n)
kernel_name = 'mk_lm_tower_d2_tok_ids256_r4_5f1791'

def setup_inputs(seed: int=0):
    np.random.seed(seed)
    _w = jnp.asarray

    def _rec_inputs():
        import jax
        import jax.numpy as jnp
        _rk = jax.random.key(seed)
        x = jax.random.randint(jax.random.fold_in(_rk, 1), (128, 128), 0, 25000, jnp.int32)
        fside_BS_outcomes = jax.random.uniform(jax.random.fold_in(_rk, 21), (128, 128), jnp.float32, 0.0, 0.999994)
        fside_BS_timestamps = -0.0064186 + 0.999588 * jax.random.normal(jax.random.fold_in(_rk, 22), (128, 128), jnp.float32)
        return (x, fside_BS_outcomes, fside_BS_timestamps)
    x, fside_BS_outcomes, fside_BS_timestamps = _rec_inputs()

    def _L0_tok_setup():
        import jax, jax.numpy as jnp
        import numpy as np
        N_Q = 25000
        D = 64
        B, L = (32, 512)
        LN_EPS = 1e-05
        key = jax.random.key(seed)
        ks = jax.random.split(key, 6)
        q_idx = jax.random.randint(ks[0], (B, L), 0, N_Q, dtype=jnp.int64) if jax.config.jax_enable_x64 else jax.random.randint(ks[0], (B, L), 0, N_Q, dtype=jnp.int32)
        outcomes = jax.random.uniform(ks[1], (B, L), dtype=jnp.float32)
        timestamps = jax.random.normal(ks[2], (B, L), dtype=jnp.float32)
        h_q = jax.random.normal(ks[3], (N_Q, D), dtype=jnp.float32)
        bound = float(np.sqrt(6.0 / (D + 2 + D)))
        W_proj_w = jax.random.uniform(ks[4], (D, D + 2), minval=-bound, maxval=bound, dtype=jnp.float32)
        W_proj_b = jnp.zeros((D,), jnp.float32)
        return {'q_idx': q_idx, 'outcomes': outcomes, 'timestamps': timestamps, 'h_q': h_q, 'W_o': jnp.ones((1,), jnp.float32), 'W_dt': jnp.ones((1,), jnp.float32), 'W_proj_w': W_proj_w, 'W_proj_b': W_proj_b, 'ln_g': jnp.ones((D,), jnp.float32), 'ln_b': jnp.zeros((D,), jnp.float32)}
    _L0_tok_all = _L0_tok_setup()
    _L0_tok_in = {k: v for k, v in _L0_tok_all.items() if k in ('h_q', 'W_o', 'W_dt', 'W_proj_w', 'W_proj_b', 'ln_g', 'ln_b')}
    del _L0_tok_all

    def _L0_attn_setup():
        import jax, jax.numpy as jnp
        import numpy as np
        U_DECAY = 0.97
        X_DECAY = 0.97
        LN_EPS = 1e-05
        L1_EPS = 1e-12

        def _ln(x):
            m = jnp.mean(x, axis=-1, keepdims=True)
            v = jnp.mean((x - m) ** 2, axis=-1, keepdims=True)
            return (x - m) * jax.lax.rsqrt(v + LN_EPS)
        key = jax.random.key(seed)
        k0, k1, k2, k3 = jax.random.split(key, 4)
        B, T, d, n = (8, 64, 64, 256)
        embeddings = jax.random.normal(k0, (B, T, d), dtype=jnp.float32)
        E = jax.random.normal(k1, (d, n), dtype=jnp.float32) / n ** 0.5
        Dx = jax.random.normal(k2, (n, d), dtype=jnp.float32) / d ** 0.5
        Dy = jax.random.normal(k3, (n, d), dtype=jnp.float32) / d ** 0.5
        return {'embeddings': embeddings, 'E': E, 'Dx': Dx, 'Dy': Dy}
    _L0_attn_all = _L0_attn_setup()
    _L0_attn_in = {k: v for k, v in _L0_attn_all.items() if k in ('E', 'Dx', 'Dy')}
    del _L0_attn_all

    def _L0_ffn_setup():
        import jax, jax.numpy as jnp
        import numpy as np
        E = 8
        K = 2
        D = 64
        H = 128
        DOUT = 64
        EPS = 1e-05
        key = jax.random.key(seed)
        ks = jax.random.split(key, 9)
        s = 0.02
        return {'x': jax.random.normal(ks[0], (4, 2048, D), jnp.float32), 'gamma': 1.0 + 0.05 * jax.random.normal(ks[1], (D,), jnp.float32), 'beta': 0.05 * jax.random.normal(ks[2], (D,), jnp.float32), 'Wr': 0.01 * jax.random.normal(ks[3], (D, E), jnp.float32), 'br': jnp.zeros((E,), jnp.float32), 'W1': s * jax.random.normal(ks[4], (E, D, H), jnp.float32), 'b1': s * jax.random.normal(ks[5], (E, H), jnp.float32), 'W2': s * jax.random.normal(ks[6], (E, H, DOUT), jnp.float32), 'b2': s * jax.random.normal(ks[7], (E, DOUT), jnp.float32)}
    _L0_ffn_all = _L0_ffn_setup()
    _L0_ffn_in = {k: v for k, v in _L0_ffn_all.items() if k in ('gamma', 'beta', 'Wr', 'br', 'W1', 'b1', 'W2', 'b2')}
    del _L0_ffn_all

    def _L1_attn_setup():
        import jax, jax.numpy as jnp
        import numpy as np
        import math
        B, S, D = (4, 1024, 64)
        key = jax.random.key(seed)
        ks = jax.random.split(key, 9)
        s = 1.0 / math.sqrt(D)
        return {'src': jax.random.normal(ks[0], (B, S, D), dtype=jnp.float32), 'Wq': jax.random.normal(ks[1], (D, D), dtype=jnp.float32) * s, 'bq': jax.random.normal(ks[2], (D,), dtype=jnp.float32) * s, 'Wk': jax.random.normal(ks[3], (D, D), dtype=jnp.float32) * s, 'bk': jax.random.normal(ks[4], (D,), dtype=jnp.float32) * s, 'Wv': jax.random.normal(ks[5], (D, D), dtype=jnp.float32) * s, 'bv': jax.random.normal(ks[6], (D,), dtype=jnp.float32) * s, 'Wo': jax.random.normal(ks[7], (D, D), dtype=jnp.float32) * s, 'bo': jax.random.normal(ks[8], (D,), dtype=jnp.float32) * s}
    _L1_attn_all = _L1_attn_setup()
    _L1_attn_in = {k: v for k, v in _L1_attn_all.items() if k in ('Wq', 'bq', 'Wk', 'bk', 'Wv', 'bv', 'Wo', 'bo')}
    del _L1_attn_all

    def _L1_ffn_setup():
        import jax, jax.numpy as jnp
        import numpy as np
        TOP_K = 2
        key = jax.random.key(seed)
        ks = jax.random.split(key, 4)
        B, L, D, H, E = (8, 1024, 64, 256, 8)
        s = 0.02
        return {'x': jax.random.normal(ks[0], (B, L, D), jnp.float32), 'Wg': jax.random.normal(ks[1], (D, E), jnp.float32) * s, 'bg': jnp.zeros((E,), jnp.float32), 'W1': jax.random.normal(ks[2], (E, D, H), jnp.float32) * s, 'b1': jnp.zeros((E, H), jnp.float32), 'W2': jax.random.normal(ks[3], (E, H, D), jnp.float32) * s, 'b2': jnp.zeros((E, D), jnp.float32)}
    _L1_ffn_all = _L1_ffn_setup()
    _L1_ffn_in = {k: v for k, v in _L1_ffn_all.items() if k in ('Wg', 'bg', 'W1', 'b1', 'W2', 'b2')}
    del _L1_ffn_all
    return {'x': x, 'fside_BS_outcomes': fside_BS_outcomes, 'fside_BS_timestamps': fside_BS_timestamps, 'L0_tok_h_q': _L0_tok_in['h_q'], 'L0_tok_W_o': _L0_tok_in['W_o'], 'L0_tok_W_dt': _L0_tok_in['W_dt'], 'L0_tok_W_proj_w': _L0_tok_in['W_proj_w'], 'L0_tok_W_proj_b': _L0_tok_in['W_proj_b'], 'L0_tok_ln_g': _L0_tok_in['ln_g'], 'L0_tok_ln_b': _L0_tok_in['ln_b'], 'L0_attn_E': _L0_attn_in['E'], 'L0_attn_Dx': _L0_attn_in['Dx'], 'L0_attn_Dy': _L0_attn_in['Dy'], 'L0_ffn_gamma': _L0_ffn_in['gamma'], 'L0_ffn_beta': _L0_ffn_in['beta'], 'L0_ffn_Wr': _L0_ffn_in['Wr'], 'L0_ffn_br': _L0_ffn_in['br'], 'L0_ffn_W1': _L0_ffn_in['W1'], 'L0_ffn_b1': _L0_ffn_in['b1'], 'L0_ffn_W2': _L0_ffn_in['W2'], 'L0_ffn_b2': _L0_ffn_in['b2'], 'L1_attn_Wq': _L1_attn_in['Wq'], 'L1_attn_bq': _L1_attn_in['bq'], 'L1_attn_Wk': _L1_attn_in['Wk'], 'L1_attn_bk': _L1_attn_in['bk'], 'L1_attn_Wv': _L1_attn_in['Wv'], 'L1_attn_bv': _L1_attn_in['bv'], 'L1_attn_Wo': _L1_attn_in['Wo'], 'L1_attn_bo': _L1_attn_in['bo'], 'L1_ffn_Wg': _L1_ffn_in['Wg'], 'L1_ffn_bg': _L1_ffn_in['bg'], 'L1_ffn_W1': _L1_ffn_in['W1'], 'L1_ffn_b1': _L1_ffn_in['b1'], 'L1_ffn_W2': _L1_ffn_in['W2'], 'L1_ffn_b2': _L1_ffn_in['b2']}

def reference(x, fside_BS_outcomes, fside_BS_timestamps, L0_tok_h_q, L0_tok_W_o, L0_tok_W_dt, L0_tok_W_proj_w, L0_tok_W_proj_b, L0_tok_ln_g, L0_tok_ln_b, L0_attn_E, L0_attn_Dx, L0_attn_Dy, L0_ffn_gamma, L0_ffn_beta, L0_ffn_Wr, L0_ffn_br, L0_ffn_W1, L0_ffn_b1, L0_ffn_W2, L0_ffn_b2, L1_attn_Wq, L1_attn_bq, L1_attn_Wk, L1_attn_bk, L1_attn_Wv, L1_attn_bv, L1_attn_Wo, L1_attn_bo, L1_ffn_Wg, L1_ffn_bg, L1_ffn_W1, L1_ffn_b1, L1_ffn_W2, L1_ffn_b2):
    import jax
    import jax.numpy as jnp

    def _L0_tok_ref(q_idx, outcomes, timestamps, h_q, W_o, W_dt, W_proj_w, W_proj_b, ln_g, ln_b):
        import jax, jax.numpy as jnp
        import numpy as np
        N_Q = 25000
        D = 64
        B, L = (32, 512)
        LN_EPS = 1e-05
        idx = jnp.clip(q_idx, 0, h_q.shape[0] - 1)
        q_emb = h_q[idx]
        o_feat = jnp.clip(outcomes[..., None] * W_o, -5.0, 5.0)
        t_feat = jnp.clip(jnp.log1p(jnp.abs(timestamps))[..., None] * W_dt, -5.0, 5.0)
        x = jnp.concatenate([q_emb, o_feat, t_feat], axis=-1)
        h = jnp.einsum('bli,oi->blo', x, W_proj_w) + W_proj_b
        mu = jnp.mean(h, axis=-1, keepdims=True)
        var = jnp.mean(jnp.square(h - mu), axis=-1, keepdims=True)
        return (h - mu) * jax.lax.rsqrt(var + LN_EPS) * ln_g + ln_b

    def _L0_attn_ref(embeddings, E, Dx, Dy):
        import jax, jax.numpy as jnp
        import numpy as np
        U_DECAY = 0.97
        X_DECAY = 0.97
        LN_EPS = 1e-05
        L1_EPS = 1e-12

        def _ln(x):
            m = jnp.mean(x, axis=-1, keepdims=True)
            v = jnp.mean((x - m) ** 2, axis=-1, keepdims=True)
            return (x - m) * jax.lax.rsqrt(v + LN_EPS)
        B, T, d = embeddings.shape
        n = E.shape[1]

        def step(carry, v_prev):
            x_state, rho = carry
            x_update = jax.nn.relu(v_prev @ Dx.T)
            x_t = X_DECAY * x_state + x_update
            x_t = x_t / jnp.maximum(jnp.sum(jnp.abs(x_t), axis=-1, keepdims=True), L1_EPS)
            a_star = jnp.einsum('bdn,bn->bd', rho, x_t)
            y_core = _ln(a_star) @ Dy.T
            y_t = jax.nn.relu(y_core) * jax.nn.relu(x_t)
            v_star = _ln(y_t @ E.T)
            rho_t = U_DECAY * rho + _ln(v_prev)[:, :, None] * x_t[:, None, :]
            return ((x_t, rho_t), v_star)
        x0 = jnp.zeros((B, n), dtype=embeddings.dtype)
        rho0 = jnp.zeros((B, d, n), dtype=embeddings.dtype)
        _, vs = jax.lax.scan(step, (x0, rho0), jnp.swapaxes(embeddings, 0, 1))
        return jnp.swapaxes(vs, 0, 1)

    def _L0_ffn_ref(x, gamma, beta, Wr, br, W1, b1, W2, b2):
        import jax, jax.numpy as jnp
        import numpy as np
        E = 8
        K = 2
        D = 64
        H = 128
        DOUT = 64
        EPS = 1e-05
        mu = jnp.mean(x, axis=-1, keepdims=True)
        var = jnp.mean(jnp.square(x - mu), axis=-1, keepdims=True)
        xn = (x - mu) * jax.lax.rsqrt(var + EPS) * gamma + beta
        logits = jnp.einsum('bsd,de->bse', xn, Wr) + br
        top_vals, top_idx = jax.lax.top_k(logits, K)
        w = jax.nn.softmax(top_vals, axis=-1)
        w_full = jnp.einsum('bsk,bske->bse', w, jax.nn.one_hot(top_idx, E, dtype=w.dtype))
        y = jnp.zeros(x.shape[:-1] + (DOUT,), x.dtype)
        for e in range(E):
            h = jax.nn.gelu(jnp.einsum('bsd,dh->bsh', xn, W1[e]) + b1[e], approximate=False)
            y_e = jnp.einsum('bsh,hd->bsd', h, W2[e]) + b2[e]
            y = y + y_e * w_full[..., e, None]
        return y

    def _L1_attn_ref(src, Wq, bq, Wk, bk, Wv, bv, Wo, bo):
        import jax, jax.numpy as jnp
        import numpy as np
        import math
        B, S, D = (4, 1024, 64)
        q = src @ Wq.T + bq
        k = src @ Wk.T + bk
        v = src @ Wv.T + bv
        row_mask = (q[:, :, 0] != 0) & (k[:, :, 0] != 0)
        mask = row_mask[:, :, None]
        scale = 1.0 / math.sqrt(D)
        scores = jnp.einsum('bid,bjd->bij', q, k) * scale
        scores = jnp.where(mask, scores, jnp.float32(-1000000000.0))
        prob = jax.nn.softmax(scores, axis=-1)
        prob = jnp.where(mask, prob, 0.0)
        out = jnp.einsum('bij,bjd->bid', prob, v)
        return out @ Wo.T + bo

    def _L1_ffn_ref(x, Wg, bg, W1, b1, W2, b2):
        import jax, jax.numpy as jnp
        import numpy as np
        TOP_K = 2
        B, L, D = x.shape
        E = W1.shape[0]
        xf = x.reshape(-1, D)
        gate_logits = xf @ Wg + bg
        top_w, top_i = jax.lax.top_k(gate_logits, TOP_K)
        top_w = jax.nn.softmax(top_w, axis=-1)
        w_dense = jnp.sum(jax.nn.one_hot(top_i, E, dtype=xf.dtype) * top_w[..., None], axis=1)
        out = jnp.zeros_like(xf)
        for e in range(E):
            h = jax.nn.gelu(xf @ W1[e] + b1[e], approximate=False)
            out = out + w_dense[:, e:e + 1] * (h @ W2[e] + b2[e])
        return out.reshape(B, L, D)
    h = _L0_tok_ref(x, fside_BS_outcomes, fside_BS_timestamps, L0_tok_h_q, L0_tok_W_o, L0_tok_W_dt, L0_tok_W_proj_w, L0_tok_W_proj_b, L0_tok_ln_g, L0_tok_ln_b)
    h = h + _L0_attn_ref(_layernorm(h, axis=-1), L0_attn_E, L0_attn_Dx, L0_attn_Dy)
    h = h + _L0_ffn_ref(_layernorm(h, axis=-1), L0_ffn_gamma, L0_ffn_beta, L0_ffn_Wr, L0_ffn_br, L0_ffn_W1, L0_ffn_b1, L0_ffn_W2, L0_ffn_b2)
    h = h + _L1_attn_ref(_layernorm(h, axis=-1), L1_attn_Wq, L1_attn_bq, L1_attn_Wk, L1_attn_bk, L1_attn_Wv, L1_attn_bv, L1_attn_Wo, L1_attn_bo)
    h = h + _L1_ffn_ref(_layernorm(h, axis=-1), L1_ffn_Wg, L1_ffn_bg, L1_ffn_W1, L1_ffn_b1, L1_ffn_W2, L1_ffn_b2)
    return h

_drawn_inputs = setup_inputs


def setup_inputs(seed=0):
    import zlib

    import numpy as np

    out = dict(_drawn_inputs(seed))
    spreads = {'L0_tok_W_proj_b': (0.0, 0.1),
     'L0_tok_ln_g': (1.0, 0.2),
     'L0_tok_ln_b': (0.0, 0.1),
     'L0_ffn_br': (0.0, 0.421),
     'L1_ffn_bg': (0.0, 0.1),
     'L1_ffn_b1': (0.0, 0.8),
     'L1_ffn_b2': (0.0, 0.523)}
    factors = {'L0_ffn_gamma': 8.0,
     'L0_ffn_beta': 8.0,
     'L0_ffn_Wr': 7.906,
     'L0_ffn_W1': 5.075,
     'L0_ffn_b1': 8.0,
     'L0_ffn_W2': 4.976,
     'L0_ffn_b2': 4.379,
     'L1_attn_bq': 9.048,
     'L1_attn_bk': 64.0,
     'L1_ffn_W1': 4.137,
     'L1_ffn_W2': 3.534}
    for name, (base, spread) in spreads.items():
        noise = np.random.default_rng([zlib.crc32(name.encode()), seed]).standard_normal(out[name].shape)
        drawn = base * np.exp(spread * noise) if base else spread * noise
        out[name] = jnp.asarray(drawn.astype(out[name].dtype))
    for name, factor in factors.items():
        out[name] = (out[name] * factor).astype(out[name].dtype)
    return out
```

```python
from contextlib import ExitStack

import concourse.bass as bass
from concourse import mybir

ALU = mybir.AluOpType
ACT = mybir.ActivationFunctionType
AX = mybir.AxisListType
F32 = mybir.dt.float32
F32R = mybir.dt.float32r
I32 = mybir.dt.int32
U32 = mybir.dt.uint32

P = 128
G = 4
D = 64
N = 256
NCH = N // P
NE = 8
GT = G * P
EPS = 1e-5
DECAY = 0.97
TINY = 1e-12
LAYERS = 2


class Order:

    def __init__(self, eng, sem):
        self.eng, self.sem, self.n = eng, sem, 0

    def one(self):
        self.n += 1
        return 1

    def restart(self):
        if self.n:
            self.eng.wait_ge(self.sem, self.n)
            self.eng.sem_clear(self.sem)
            self.n = 0


class Weights:
    pass


def tower(nc, a, out):
    B = a["x"].shape[0]
    NG = B // G
    TOK = B * P
    NQ = a["L0_tok_h_q"].shape[0]
    H1 = a["L1_ffn_W1"].shape[2]
    ctx = ExitStack()
    with ctx:
        def sb(name, shape, dt=F32):
            return ctx.enter_context(nc.sbuf_tensor(name, shape, dt))

        def ps(name, shape):
            return ctx.enter_context(nc.psum_tensor(name, shape, F32))

        def sem(name):
            return ctx.enter_context(nc.semaphore(name))

        w = Weights()
        w.h_all = sb("h_all", [P, B, D])
        w.gates = [nc.dram_tensor(f"gates{layer}", (NE, TOK), F32).ap() for layer in range(2)]
        w.ident = sb("ident", [P, P])
        w.mhalf, w.eps = sb("mhalf", [P, G]), sb("eps", [P, G])
        w.iota_e = sb("iota_e", [P, NE])
        w.idx_all = sb("idx_all", [P, B], I32)
        w.feat_all = sb("feat_all", [P, B, 2])
        w.wproj = sb("wproj", [D + 3, D])
        w.dx_hi, w.dx_lo = sb("dx_hi", [P, N], F32R), sb("dx_lo", [P, N], F32R)
        w.dy_hi, w.dy_lo = sb("dy_hi", [P, N], F32R), sb("dy_lo", [P, N], F32R)
        w.et = sb("et", [P, NCH, D])
        w.decay = sb("decay", [P, P])
        w.sel_in = sb("sel_in", [P, G, G])
        w.sel_out = sb("sel_out", [G, G, P])
        w.lng, w.lnb = sb("lng", [P, D]), sb("lnb", [P, D])
        w.f0_w1_hi, w.f0_w1_lo = sb("f0_w1_hi", [P, NE * P], F32R), sb("f0_w1_lo", [P, NE * P], F32R)
        w.f0_w2 = sb("f0_w2", [P, NE, 1, D])
        w.f0_b1 = sb("f0_b1", [P, NE, 1])
        w.f0_b2 = sb("f0_b2", [P, NE // 2])
        w.f0_wr, w.f0_br = sb("f0_wr", [P, NE]), sb("f0_br", [P, NE])
        C1 = H1 // P
        w.f1_w1_hi, w.f1_w1_lo = sb("f1_w1_hi", [P, NE * H1], F32R), sb("f1_w1_lo", [P, NE * H1], F32R)
        w.f1_w2 = sb("f1_w2", [P, NE, C1, D])
        w.f1_b1 = sb("f1_b1", [P, NE, C1])
        w.f1_b2 = sb("f1_b2", [P, NE // 2])
        w.f1_wr, w.f1_br = sb("f1_wr", [P, NE]), sb("f1_br", [P, NE])
        w.wqk_hi, w.wqk_lo = sb("wqk_hi", [P, P], F32R), sb("wqk_lo", [P, P], F32R)
        w.bqk = sb("bqk", [P, 1])
        w.wv2 = sb("wv2", [P, D + 2])
        w.bv2 = sb("bv2", [P, D + 2])
        w.bo = sb("bo", [P, D])

        with ExitStack() as stage:
            _setup(nc, a, w, B, NQ, stage)
        nc.all_engine_barrier()
        with ExitStack() as stage:
            _layer0(nc, a, w, NG, stage, None if LAYERS == 2 else out)
        if LAYERS == 2:
            nc.all_engine_barrier()
            with ExitStack() as stage:
                _layer1(nc, a, w, NG, stage, out)


def _setup(nc, a, w, B, NQ, stage):
    def sb(name, shape, dt=F32):
        return stage.enter_context(nc.sbuf_tensor(name, shape, dt))

    def sem(name):
        return stage.enter_context(nc.semaphore(name))

    bank = [stage.enter_context(nc.psum_tensor(f"st_bank{i}", [P, 512], F32)) for i in range(7)]
    natural = sb("st_natural", [P, 3, B])
    idx_raw = sb("st_idx", [B, P], I32)
    logt = sb("st_logt", [P, B])
    wproj_n = sb("st_wproj", [D, D + 2])
    dx2 = sb("st_dx2", [P, NCH, 2 * D])
    dy2 = sb("st_dy2", [P, NCH, 2 * D])
    e_n = sb("st_e", [D, N])
    wqk2 = sb("st_wqk2", [P, 2 * D])
    wo_n, wvb = sb("st_wo", [D, D]), sb("st_wvb", [D, 2 * (D + 1)])
    wo_t = sb("st_wo_t", [D, D])
    scale_b = sb("st_scale_b", [P, D])
    w1a = sb("st_w1a", [P, NE * P])
    w1b = sb("st_w1b", [P, NE * 2 * P])
    gamma, beta = sb("st_gamma", [P, 1]), sb("st_beta", [P, 1])
    beta_b = sb("st_beta_b", [D, P])
    wr0, wr1 = sb("st_wr0", [P, NE]), sb("st_wr1", [P, NE])
    bq0 = sb("st_bq0", [P, 2])
    w_feat = sb("st_w_feat", [P, 2])
    lnmask = sb("st_lnmask", [P, P])
    slot = sb("st_slot", [P, P])
    w_full = sb("st_w_full", [P, P])
    loaded, made, moved = sem("st_loaded"), sem("st_made"), sem("st_moved")
    built, order, a_order, g_order = sem("st_built"), sem("st_order"), sem("st_a_order"), sem("st_g_order")
    H1C = w.f1_w2.shape[2]

    def row(ap, n):
        return ap.rearrange("(o d) -> o d", o=1).broadcast_to([n, ap.shape[0]])

    def col(ap):
        return ap.rearrange("(d o) -> d o", o=1)

    loads = [
        (idx_raw[:], a["x"]),
        (natural[:, 1, :], a["fside_BS_outcomes"]),
        (natural[:, 2, :], a["fside_BS_timestamps"]),
        (wproj_n[:], a["L0_tok_W_proj_w"]),
        (w_feat[:, 0:1], row(a["L0_tok_W_o"], P)), (w_feat[:, 1:2], row(a["L0_tok_W_dt"], P)),
        (w.wproj[D + 2:D + 3, :], a["L0_tok_W_proj_b"].rearrange("(o d) -> o d", o=1)),
        (w.lng[:], row(a["L0_tok_ln_g"], P)), (w.lnb[:], row(a["L0_tok_ln_b"], P)),
        (dx2[:, :, 0:D], a["L0_attn_Dx"].rearrange("(c p) d -> p c d", p=P)),
        (dx2[:, :, D:2 * D], a["L0_attn_Dx"].rearrange("(c p) d -> p c d", p=P)),
        (dy2[:, :, 0:D], a["L0_attn_Dy"].rearrange("(c p) d -> p c d", p=P)),
        (dy2[:, :, D:2 * D], a["L0_attn_Dy"].rearrange("(c p) d -> p c d", p=P)),
        (e_n[:], a["L0_attn_E"]),
        (wqk2[0:D, 0:D], a["L1_attn_Wq"]), (wqk2[0:D, D:2 * D], a["L1_attn_Wq"]),
        (wqk2[D:P, 0:D], a["L1_attn_Wk"]), (wqk2[D:P, D:2 * D], a["L1_attn_Wk"]),
        (w.bqk[0:D, :], col(a["L1_attn_bq"])), (w.bqk[D:P, :], col(a["L1_attn_bk"])),
        (wo_n[:], a["L1_attn_Wo"]),
        (wvb[:, 0:D], a["L1_attn_Wv"]), (wvb[:, D:2 * D], a["L1_attn_Wv"]),
        (scale_b[0:D, 0:1], col(a["L1_attn_bv"])),
        (w.bo[:], row(a["L1_attn_bo"], P)),
        (bq0[:, 0:1], row(a["L1_attn_bq"][0:1], P)), (bq0[:, 1:2], row(a["L1_attn_bk"][0:1], P)),
        (gamma[0:D, :], col(a["L0_ffn_gamma"])), (gamma[D:P, :], col(a["L0_ffn_gamma"])),
        (beta[0:D, :], col(a["L0_ffn_beta"])),
        (wr0[0:D, :], a["L0_ffn_Wr"]), (wr0[D:P, :], a["L0_ffn_Wr"]),
        (w.f1_wr[0:D, :], a["L1_ffn_Wg"]), (w.f1_wr[D:P, :], a["L1_ffn_Wg"]),
        (w.f0_br[:], row(a["L0_ffn_br"], P)), (w.f1_br[:], row(a["L1_ffn_bg"], P)),
        (w.f0_w2[:, :, 0, :], a["L0_ffn_W2"].rearrange("e h d -> h e d")),
        (w.f0_b1[:, :, 0], a["L0_ffn_b1"].rearrange("e h -> h e")),
    ]
    for half in range(2):
        rows = slice(half * D, half * D + D)
        loads += [
            (w1a[rows, :].rearrange("d (e h) -> d e h", e=NE), a["L0_ffn_W1"].rearrange("e d h -> d e h")),
            (w1b[rows, :].rearrange("d (e h) -> d e h", e=NE), a["L1_ffn_W1"].rearrange("e d h -> d e h")),
            (w.f0_b2[rows, :], a["L0_ffn_b2"].rearrange("(p two) d -> two d p", two=2)[half]),
            (w.f1_b2[rows, :], a["L1_ffn_b2"].rearrange("(p two) d -> two d p", two=2)[half]),
        ]
    for c in range(H1C):
        loads += [
            (w.f1_w2[:, :, c, :], a["L1_ffn_W2"].rearrange("e (c h) d -> c h e d", c=H1C)[c]),
            (w.f1_b1[:, :, c], a["L1_ffn_b1"].rearrange("e (c h) -> c h e", c=H1C)[c]),
        ]
    ALL = 16 * len(loads)

    with nc.Block() as block:
        @block.sync
        def _(sp):
            with nc.allow_non_contiguous_dma(reason="small weights, once"):
                for dst, src in loads[0::2]:
                    sp.dma_start(dst, src).then_inc(loaded, 16)

        @block.gpsimd
        def _(pool):
            own = Order(pool, g_order)
            nc.gpsimd.memset(w.ident[:], 1.0).then_inc(g_order, own.one())
            nc.gpsimd.memset(w.sel_in[:], 1.0).then_inc(g_order, own.one())
            nc.gpsimd.memset(w.sel_out[:], 1.0).then_inc(g_order, own.one())
            nc.gpsimd.memset(w.mhalf[:], -0.5).then_inc(g_order, own.one())
            nc.gpsimd.memset(w.eps[:], EPS).then_inc(g_order, own.one())
            nc.gpsimd.iota(w.iota_e[:], pattern=[[1, NE]], base=0, channel_multiplier=0,
                           allow_small_or_imprecise_dtypes=True).then_inc(g_order, own.one())
            nc.gpsimd.iota(lnmask[:], pattern=[[1, P]], base=-1, channel_multiplier=-1,
                           allow_small_or_imprecise_dtypes=True).then_inc(g_order, own.one())
            nc.gpsimd.memset(slot[:], DECAY).then_inc(g_order, own.one())
            pool.wait_ge(g_order, own.n)
            nc.gpsimd.affine_select(out=w.ident[:], in_=w.ident[:], compare_op=ALU.is_equal, fill=0.0,
                                    base=0, pattern=[[-1, P]], channel_multiplier=1).then_inc(g_order, own.one())
            nc.gpsimd.affine_select(out=w.sel_in[:], in_=w.sel_in[:], compare_op=ALU.is_equal, fill=0.0,
                                    base=0, pattern=[[1, G], [-1, G]], channel_multiplier=0).then_inc(g_order, own.one())
            nc.gpsimd.affine_select(out=w.sel_out[:], in_=w.sel_out[:], compare_op=ALU.is_equal,
                                    fill=0.0, base=0, pattern=[[-1, G], [0, P]], channel_multiplier=1).then_inc(g_order, own.one())
            nc.gpsimd.tensor_scalar(w_full[:], lnmask[:], 0.0, None, ALU.max).then_inc(g_order, own.one())
            pool.wait_ge(g_order, own.n)
            nc.gpsimd.tensor_tensor(slot[:], slot[:], w_full[:], ALU.pow).then_inc(g_order, own.one())
            pool.wait_ge(g_order, own.n)
            nc.gpsimd.affine_select(out=w.decay[:], in_=slot[:], compare_op=ALU.is_ge, fill=0.0,
                                    base=-1, pattern=[[1, P]], channel_multiplier=-1).then_inc(made, 1)

        @block.tensor
        def _(pe):
            pe.wait_ge(loaded, ALL)
            pe.wait_ge(made, 1)
            pe.wait_ge(built, 1)
            idn, idd = w.ident[:], w.ident[0:D, 0:D]
            for k in range(3):
                nc.tensor.transpose(bank[6 if k == 2 else 0][:, k * P:(k + 1) * P], natural[:, k, :], idn)
            for c in range(NCH):
                nc.tensor.transpose(bank[1][:, c * P:(c + 1) * P], dx2[:, c, :], idn)
                nc.tensor.transpose(bank[1][:, (2 + c) * P:(3 + c) * P], dy2[:, c, :], idn)
                nc.tensor.transpose(bank[2][:, c * D:(c + 1) * D], e_n[:, c * P:(c + 1) * P], idd)
            nc.tensor.transpose(bank[2][0:D + 2, P:P + D], wproj_n[:], idd)
            nc.tensor.transpose(bank[3][:, 0:P], wqk2[:], idn)
            nc.tensor.transpose(bank[3][0:D, P:P + D], wo_n[:], idd).then_inc(moved, 1)
            for e in range(NE):
                nc.tensor.matmul(bank[4][:, e:e + 1], w1a[0:D, e * P:(e + 1) * P], beta[0:D, :], start=True, stop=True)
            nc.tensor.matmul(bank[4][:, NE:2 * NE], beta_b[:], wr0[0:D, :], start=True, stop=True).then_inc(moved, 1)
            pe.wait_ge(built, 2)
            nc.tensor.matmul(bank[5][:, 0:D], wvb[:, 0:2 * D], wo_t[:], start=True, stop=True)
            nc.tensor.matmul(bank[5][:, D:2 * D], beta_b[:], wo_t[:], start=True, stop=True).then_inc(moved, 1)

        @block.scalar
        def _(act):
            with nc.allow_non_contiguous_dma(reason="small weights, once"):
                for dst, src in loads[1::2]:
                    act.dma_start(dst, src).then_inc(loaded, 16)
            act.wait_ge(moved, 1)
            own = Order(act, a_order)
            nc.scalar.activation(logt[:], bank[6][:, 2 * P:3 * P], ACT.Abs).then_inc(a_order, own.one())
            act.wait_ge(a_order, own.n)
            nc.scalar.activation(w.feat_all[:, :, 1], logt[:], ACT.Ln, bias=1.0).then_inc(a_order, own.one())
            act.wait_ge(a_order, own.n)
            nc.scalar.activation(logt[:, 0:1], logt[:, 0:1], ACT.Copy).then_inc(made, 1)

        @block.vector
        def _(dve):
            own = Order(dve, order)
            dve.wait_ge(loaded, ALL)
            nc.vector.tensor_copy(beta_b[:], beta[0:D, 0:1].to_broadcast([D, P])).then_inc(order, own.one())
            dve.wait_ge(order, own.n)
            nc.vector.tensor_copy(natural[:, 0, :], idx_raw[:]).then_inc(built, 1)
            nc.vector.tensor_scalar(w.f0_wr[:], wr0[:], gamma[:, 0:1], None, ALU.mult).then_inc(order, own.one())
            nc.vector.tensor_copy(w.f1_w1_hi[:], w1b[:]).then_inc(order, own.one())
            dve.wait_ge(order, own.n)
            nc.vector.tensor_tensor(w.f1_w1_lo[:], w1b[:], w.f1_w1_hi[:].bitcast(F32), ALU.subtract).then_inc(order, own.one())
            dve.wait_ge(moved, 1)
            nc.vector.tensor_scalar(w.idx_all[:], bank[0][:, 0:P], 0.0, float(NQ - 1), ALU.max, ALU.min).then_inc(order, own.one())
            nc.vector.tensor_copy(w.feat_all[:, :, 0], bank[0][:, P:2 * P]).then_inc(order, own.one())
            for src, hi, lo in ((bank[1][:, 0:N], w.dx_hi, w.dx_lo), (bank[1][:, N:2 * N], w.dy_hi, w.dy_lo),
                                (bank[3][:, 0:P], w.wqk_hi, w.wqk_lo)):
                nc.vector.tensor_copy(hi[:], src).then_inc(order, own.one())
                dve.wait_ge(order, own.n)
                nc.vector.tensor_tensor(lo[:], src, hi[:].bitcast(F32), ALU.subtract).then_inc(order, own.one())
            nc.vector.tensor_copy(w.et[:], bank[2][:, 0:P].rearrange("p (c d) -> p c d", c=NCH)).then_inc(order, own.one())
            nc.vector.tensor_copy(w.wproj[0:D + 2, :], bank[2][0:D + 2, P:P + D]).then_inc(order, own.one())
            nc.vector.tensor_copy(w.wv2[:, D:D + 1], bank[3][:, 0:1]).then_inc(order, own.one())
            nc.vector.tensor_copy(w.wv2[:, D + 1:D + 2], bank[3][:, D:D + 1]).then_inc(order, own.one())
            nc.vector.tensor_copy(wo_t[:], bank[3][0:D, P:P + D]).then_inc(order, own.one())
            dve.wait_ge(moved, 2)
            nc.vector.tensor_copy(beta_b[:], scale_b[0:D, 0:1].to_broadcast([D, P])).then_inc(order, own.one())
            dve.wait_ge(order, own.n)
            nc.vector.tensor_copy(w.bv2[:, D:D + 2], bq0[:]).then_inc(built, 1)
            nc.vector.tensor_tensor(w.f0_b1[:, :, 0], bank[4][:, 0:NE], w.f0_b1[:, :, 0], ALU.add).then_inc(order, own.one())
            nc.vector.tensor_tensor(w.f0_br[:], bank[4][:, NE:2 * NE], w.f0_br[:], ALU.add).then_inc(order, own.one())
            nc.vector.tensor_scalar(w1a[:], w1a[:], gamma[:, 0:1], None, ALU.mult).then_inc(order, own.one())
            dve.wait_ge(order, own.n)
            nc.vector.tensor_copy(w.f0_w1_hi[:], w1a[:]).then_inc(order, own.one())
            dve.wait_ge(order, own.n)
            nc.vector.tensor_tensor(w.f0_w1_lo[:], w1a[:], w.f0_w1_hi[:].bitcast(F32), ALU.subtract).then_inc(order, own.one())
            dve.wait_ge(moved, 3)
            nc.vector.tensor_copy(w.wv2[:, 0:D], bank[5][:, 0:D]).then_inc(order, own.one())
            nc.vector.tensor_copy(w.bv2[:, 0:D], bank[5][:, D:2 * D]).then_inc(order, own.one())
            dve.wait_ge(made, 2)
            dve.wait_ge(order, own.n)
            nc.vector.tensor_scalar(w.feat_all[:, :, 0], w.feat_all[:, :, 0], w_feat[:, 0:1], None,
                                    ALU.mult).then_inc(order, own.one())
            nc.vector.tensor_scalar(w.feat_all[:, :, 1], w.feat_all[:, :, 1], w_feat[:, 1:2], None,
                                    ALU.mult).then_inc(order, own.one())
            dve.wait_ge(order, own.n)
            nc.vector.tensor_scalar(w.feat_all[:], w.feat_all[:], -5.0, 5.0, ALU.max, ALU.min).then_inc(order, own.one())
            dve.wait_ge(order, own.n)


K = 8


def turns(eng, steps, NG, own, late=()):
    lanes = -(-steps // K)
    first = lanes - 1 + (lanes - 1) % 2

    def iteration(it, odd):
        for slot in range(K):
            for lane in sorted(range(lanes), key=lambda lane: (lane * K + slot in late, -lane)):
                g = it - lane
                if lane * K + slot < steps and not (isinstance(g, int) and not 0 <= g < NG):
                    yield lane * K + slot, g, (odd + lane) % 2
        own.restart()

    for it in range(first):
        yield from iteration(it, it % 2)
    with eng.Fori(first // 2, NG // 2) as pair:
        for u in range(2):
            yield from iteration(pair * 2 + u, u)
    for it in range(NG, NG + lanes - 1):
        yield from iteration(it, it % 2)


def some(count):
    return not (isinstance(count, int) and count <= 0)


def held(eng, value):
    return value if isinstance(value, int) else eng.snap(value)


def parity_count(g, q, each):
    return each * (g // 2 + 1) if isinstance(g, int) else g * (each // 2) + (each - q * (each // 2))


def wide(ap, n):
    return ap.unsqueeze(2).to_broadcast([ap.shape[0], ap.shape[1], n])


def rows(ap, n):
    return ap.unsqueeze(1).to_broadcast([ap.shape[0], n, ap.shape[1]])


(GATHER, _1, T1, PROJ, Z1, STATS2, E2, D2,
 T2, _9, U, _11, S, _13, R, _15,
 GRAM, _17, A, Z3, D3, T3, _22, Y,
 _24, V, H1, STATS5, V5, Z5, D5, T4,
 GATE, W, _34, WT, F0, F1, _38, F2,
 F2A, F3, F3A, F4, SUM, _45, TF) = range(47)


def _layer0(nc, a, w, NG, stage, out):
    def sb(name, shape, dt=F32):
        return stage.enter_context(nc.sbuf_tensor(name, shape, dt))

    def ps(name, shape):
        return stage.enter_context(nc.psum_tensor(name, shape, F32))

    def sem(name):
        return stage.enter_context(nc.semaphore(name))

    xin = [sb(f"xin{q}", [P, G, D + 4]) for q in range(2)]
    idx_g = sb("idx_g", [P, 2, G], I32)
    xt = sb("xt", [D + 3, GT])
    st = {k: sb(f"st{k}", [P, G, 2]) for k in range(1, 6)}
    bn = {k: sb(f"bn{k}", [P, G, 6]) for k in range(1, 6)}
    ve = {k: sb(f"ve{k}", [P, G]) for k in range(1, 6)}
    rs = {k: sb(f"rs{k}", [P, G]) for k in range(1, 6)}
    nb = {k: sb(f"nb{k}", [P, G]) for k in range(1, 6)}
    z = {k: sb(f"z{k}", [P, G, D]) for k in range(1, 6)}
    vn = {k: sb(f"vn{k}", [P, G]) for k in (2, 5)}
    rn = {k: sb(f"rn{k}", [P, G]) for k in (2, 5)}
    rr5 = sb("rr5", [P, G])
    zg = sb("zg", [P, G, D])
    h0 = sb("h0", [P, G, D])
    h1 = sb("h1", [P, G, D])
    lnv = [sb(f"lnv{q}", [P, G, D]) for q in range(2)]
    split = {k: sb(f"split{k}", [P, G, 2 * D], F32R) for k in (2, 3, 5)}
    et_in = sb("et_in", [P, GT], F32R)
    at_in = sb("at_in", [P, GT], F32R)
    xs = [sb(f"xs{q}", [P, GT], F32R) for q in range(2)]
    u = sb("u", [P, NCH, GT])
    m_c, r_c, s_c = (sb(n, [G, P]) for n in ("m_c", "r_c", "s_c"))
    sig = sb("sig", [G, P + 1])
    ab = sb("ab", [P, GT])
    d_in = sb("d_in", [P, NCH, GT])
    x = [sb(f"x{q}", [P, NCH, GT]) for q in range(2)]
    pm = sb("pm", [P, GT])
    y = sb("y", [P, NCH, GT])
    logits, top = sb("logits", [P, G, NE]), sb("top", [P, G, NE])
    ix, ixf = sb("ix", [P, G, NE], U32), sb("ixf", [P, G, 2])
    gap, th, wt2 = sb("gap", [P, G]), sb("th", [P, G]), sb("wt2", [P, G, 2])
    eq = sb("eq", [P, 2, G, NE])
    gate = sb("gate", [P, G, NE])
    gt = sb("gt", [G * NE, P])
    wb = [sb(f"wb{q}", [P, NE // 2, GT]) for q in range(2)]
    hid = sb("hid", [P, 2, 2, GT])
    part = sb("part", [P, 2, GT])
    acc = [sb(f"acc{q}", [P, GT]) for q in range(2)]

    p_t, p_tm, p_gr = ps("p_t", [P, 512]), ps("p_tm", [P, 2 * G, D]), ps("p_gr", [P, 512])
    p_u, p_h, p_y = ps("p_u", [P, NCH, GT]), ps("p_h", [P, 2, GT]), ps("p_y", [P, GT])

    gathered = [sem(f"gathered{q}") for q in range(2)]
    idx_ready, feat_ready = sem("idx_ready"), sem("feat_ready")
    t1_ready, xt_ready, proj_ready = sem("t1_ready"), sem("xt_ready"), sem("proj_ready")
    stats = {k: sem(f"stats{k}") for k in range(1, 6)}
    rstd = {k: sem(f"rstd{k}") for k in range(1, 6)}
    bias = {k: sem(f"bias{k}") for k in range(1, 6)}
    z_ready = {k: sem(f"z_ready{k}") for k in range(1, 6)}
    vn_ready = {k: sem(f"vn_ready{k}") for k in (2, 5)}
    rn_ready = {k: sem(f"rn_ready{k}") for k in (2, 5)}
    h0_ready, lnv_ready = sem("h0_ready"), sem("lnv_ready")
    split_ready = {k: sem(f"split_ready{k}") for k in (2, 3, 5)}
    t_ready = {k: sem(f"t_ready{k}") for k in (2, 3, 5)}
    in_ready = {k: sem(f"in_ready{k}") for k in (2, 3, 5)}
    u_psum, u_ready = sem("u_psum"), sem("u_ready")
    s_ready, r_ready, r_psum, ab_ready = sem("s_ready"), sem("r_ready"), sem("r_psum"), sem("ab_ready")
    x_ready, gram_ready, pm_ready, a_ready = sem("x_ready"), sem("gram_ready"), sem("pm_ready"), sem("a_ready")
    y_psum, y_ready, v_ready, h1_ready = sem("y_psum"), sem("y_ready"), sem("v_ready"), sem("h1_ready")
    logit_psum, gap_ready, th_ready = sem("logit_psum"), sem("gap_ready"), sem("th_ready")
    gate_ready, gt_psum, gt_stored = sem("gate_ready"), sem("gt_psum"), sem("gt_stored")
    wb_loaded = [sem(f"wb_loaded{q}") for q in range(2)]
    up_psum, hid_ready, down_psum = sem("up_psum"), sem("hid_ready"), sem("down_psum")
    part_ready, acc_ready, tf_ready, h2_ready = sem("part_ready"), sem("acc_ready"), sem("tf_ready"), sem("h2_ready")
    d_own, a_own, p_own, t_own, s_own = sem("d_own"), sem("a_own"), sem("p_own"), sem("t_own"), sem("s_own")
    ones_ready = sem("ones_ready")
    stored = sem("stored")

    NPAIR = NE // 2

    def ahead(g, n):
        return min(g + n, NG) if isinstance(g, int) else g + n

    def seqs(g):
        return w.h_all[:, bass.ds(g * G, G), :]

    with nc.Block() as block:
        @block.gpsimd
        def _(pool):
            own = Order(pool, p_own)
            for q in range(2):
                last = nc.gpsimd.memset(xin[q][:, :, D + 2:D + 4], 1.0)
            last.then_inc(ones_ready, 1)

            def power(k, src):
                nc.gpsimd.tensor_tensor(ve[k][:], src, w.eps[:], ALU.add).then_inc(p_own, own.one())
                pool.wait_ge(p_own, own.n)

            for step, g, q in turns(pool, TF + 1, NG, own):
                if step == GATHER:
                    if some(g - 1):
                        pool.wait_ge(t1_ready, g - 1)
                    nc.gpsimd.tensor_copy(idx_g[:, q, :], w.idx_all[:, bass.ds(g * G, G)]).then_inc(p_own, own.one())
                    nc.gpsimd.tensor_copy(xin[q][:, :, D:D + 2],
                                          w.feat_all[:, bass.ds(g * G, G), :]).then_inc(feat_ready, 1)
                    pool.wait_ge(p_own, own.n)
                    for j in range(G):
                        nc.gpsimd.indirect_dma_start(
                            out=xin[q][:, j, 0:D], out_offset=None, in_=a["L0_tok_h_q"],
                            in_offset=bass.IndirectOffsetOnAxis(ap=idx_g[:, q, j:j + 1], axis=0),
                        ).then_inc(gathered[q], 16)
                if step in (PROJ, STATS2, A, V, STATS5):
                    k = {PROJ: 1, STATS2: 2, A: 3, V: 4, STATS5: 5}[step]
                    pool.wait_ge(stats[k], g + 1)
                    power(k, st[k][:, :, 1])
                    nc.gpsimd.tensor_tensor(rs[k][:], ve[k][:], w.mhalf[:], ALU.pow).then_inc(rstd[k], 1)
                if step == Z1:
                    pool.wait_ge(z_ready[1], g + 1)
                    nc.gpsimd.tensor_tensor(zg[:], z[1][:], rows(w.lng[:], G), ALU.mult).then_inc(p_own, own.one())
                    pool.wait_ge(p_own, own.n)
                    nc.gpsimd.tensor_tensor(h0[:], zg[:], rows(w.lnb[:], G), ALU.add).then_inc(h0_ready, 1)
                if step in (E2, V5):
                    k = {E2: 2, V5: 5}[step]
                    pool.wait_ge(vn_ready[k], g + 1)
                    power(k, vn[k][:])
                    nc.gpsimd.tensor_tensor(rn[k][:], ve[k][:], w.mhalf[:], ALU.pow).then_inc(rn_ready[k], 1)
                if step == T2:
                    pool.wait_ge(z_ready[2], g + 1)
                    pool.wait_ge(rn_ready[2], g + 1)
                    nc.gpsimd.tensor_tensor(lnv[q][:], z[2][:], wide(rn[2][:], D), ALU.mult).then_inc(lnv_ready, 1)
                if step in (F2A, F3A, SUM):
                    p = {F2A: 1, F3A: 2, SUM: 3}[step]
                    pool.wait_ge(part_ready, g * NPAIR + (p + 1))
                    if p > 1:
                        pool.wait_ge(acc_ready, g * (NPAIR - 1) + (p - 1))
                    nc.gpsimd.tensor_tensor(acc[q][:], acc[q][:], part[:, p % 2, :], ALU.add).then_inc(acc_ready, 1)

        @block.tensor
        def _(pe):
            own = Order(pe, t_own)

            def transposes(src, width):
                for j in range(G):
                    last = nc.tensor.transpose(p_t[0:width, j * P:(j + 1) * P], src(j), w.ident[:])
                return last

            def stacked(dst, hi, lo, moving):
                nc.tensor.matmul(dst, hi, moving, start=True, stop=False)
                return nc.tensor.matmul(dst, lo, moving, start=False, stop=True)

            def down(g, p):
                pe.wait_ge(hid_ready, g * NE + (2 * p + 2))
                if some(g * NPAIR + p):
                    pe.wait_ge(part_ready, g * NPAIR + p)
                for half in range(2):
                    last = nc.tensor.matmul(p_y[half * D:half * D + D, :], w.f0_w2[:, 2 * p + half, 0, :],
                                            hid[:, p % 2, half, :], start=True, stop=True)
                last.then_inc(down_psum, 1)

            pe.wait_ge(ones_ready, 1)
            for step, g, q in turns(pe, TF + 1, NG, own, late=(WT, PROJ, GATE)):
                if step == T1:
                    pe.wait_ge(gathered[q], parity_count(g, q, 16 * G))
                    pe.wait_ge(feat_ready, g + 1)
                    transposes(lambda j: xin[q][:, j, 0:D + 3], D + 3).then_inc(t1_ready, 1)
                if step == PROJ:
                    pe.wait_ge(xt_ready, g + 1)
                    if some(g - 2):
                        pe.wait_ge(z_ready[4], g - 2)
                    for j in range(G):
                        last = nc.tensor.matmul(p_tm[:, j, :], xt[:, j * P:(j + 1) * P], w.wproj[:],
                                                start=True, stop=True)
                    last.then_inc(proj_ready, 1)
                if step in (T2, T3, T4):
                    k = {T2: 2, T3: 3, T4: 5}[step]
                    pe.wait_ge(split_ready[k], g + 1)
                    if step == T2 and some(g - 2):
                        pe.wait_ge(in_ready[5], g - 2)
                    if step == T4:
                        pe.wait_ge(in_ready[3], ahead(g, 2))
                        if some(g - 1):
                            pe.wait_ge(h2_ready, g - 1)
                    transposes(lambda j: split[k][:, j, :].bitcast(F32), P).then_inc(t_ready[k], 1)
                if step == U:
                    pe.wait_ge(in_ready[2], g + 1)
                    for c in range(NCH):
                        cols = slice(c * P, (c + 1) * P)
                        last = stacked(p_u[:, c, :], w.dx_hi[:, cols], w.dx_lo[:, cols], et_in[:])
                    last.then_inc(u_psum, 1)
                if step == S:
                    pe.wait_ge(u_ready, g + 1)
                    for j in range(G):
                        for c in range(NCH):
                            last = nc.tensor.matmul(p_u[0:G, 0, 0:P], w.sel_in[:, j, :], u[:, c, j * P:(j + 1) * P],
                                                    start=(j + c == 0), stop=(j == G - 1 and c == NCH - 1))
                    last.then_inc(s_ready, 1)
                if step == R:
                    pe.wait_ge(r_ready, g + 1)
                    for j in range(G):
                        last = nc.tensor.matmul(p_gr[:, j * P:(j + 1) * P], w.sel_out[:, j, :], r_c[:],
                                                start=True, stop=True)
                    last.then_inc(r_psum, 1)
                if step == GRAM:
                    pe.wait_ge(x_ready, g + 1)
                    for j in range(G):
                        tile = slice(j * P, (j + 1) * P)
                        for c in range(NCH):
                            last = nc.tensor.matmul(p_gr[:, tile], x[q][:, c, tile], x[q][:, c, tile],
                                                    start=(c == 0), stop=(c == NCH - 1))
                    last.then_inc(gram_ready, 1)
                if step == A:
                    pe.wait_ge(pm_ready, g + 1)
                    pe.wait_ge(lnv_ready, g + 1)
                    for j in range(G):
                        last = nc.tensor.matmul(p_gr[:, j * D:(j + 1) * D], pm[:, j * P:(j + 1) * P], lnv[q][:, j, :],
                                                start=True, stop=True)
                    last.then_inc(a_ready, 1)
                if step == Y:
                    pe.wait_ge(in_ready[3], g + 1)
                    for c in range(NCH):
                        cols = slice(c * P, (c + 1) * P)
                        last = stacked(p_u[:, c, :], w.dy_hi[:, cols], w.dy_lo[:, cols], at_in[:])
                    last.then_inc(y_psum, 1)
                if step == V:
                    pe.wait_ge(y_ready, g + 1)
                    if some(g):
                        pe.wait_ge(gap_ready, g)
                    for j in range(G):
                        for c in range(NCH):
                            last = nc.tensor.matmul(p_tm[:, j, :], y[:, c, j * P:(j + 1) * P], w.et[:, c, :],
                                                    start=(c == 0), stop=(c == NCH - 1))
                    last.then_inc(v_ready, 1)
                if step == GATE:
                    pe.wait_ge(in_ready[5], g + 1)
                    for j in range(G):
                        last = nc.tensor.matmul(p_tm[:, 0, j * NE:(j + 1) * NE],
                                                xs[q][:, j * P:(j + 1) * P].bitcast(F32), w.f0_wr[:],
                                                start=True, stop=True)
                    last.then_inc(logit_psum, 1)
                if step == WT:
                    pe.wait_ge(gate_ready, g + 1)
                    pe.wait_ge(u_ready, ahead(g, 4))
                    nc.tensor.transpose(p_u[0:G * NE, 1, 0:P], gate[:].rearrange("p g e -> p (g e)"),
                                        w.ident[:]).then_inc(gt_psum, 1)
                if step in (F0, F1, F2, F3, F4):
                    p = (F0, F1, F2, F3, F4).index(step)
                    if p:
                        down(g, p - 1)
                    if p < NPAIR:
                        for half in range(2):
                            cols = slice((2 * p + half) * P, (2 * p + half + 1) * P)
                            last = stacked(p_h[:, half, :], w.f0_w1_hi[:, cols], w.f0_w1_lo[:, cols], xs[q][:])
                            last.then_inc(up_psum, 1)
                if step == TF:
                    pe.wait_ge(acc_ready, g * (NPAIR - 1) + (NPAIR - 1))
                    pe.wait_ge(in_ready[3], ahead(g, 4))
                    transposes(lambda j: acc[q][:, j * P:(j + 1) * P], P).then_inc(tf_ready, 1)

        @block.scalar
        def _(act):
            own = Order(act, a_own)

            def normalise(k, src, scale, offset):
                for j in range(G):
                    last = nc.scalar.activation(z[k][:, j, :], src(j), ACT.Identity, scale=scale[:, j:j + 1],
                                                bias=offset[:, j:j + 1])
                last.then_inc(z_ready[k], 1)

            nc.scalar.activation(th[:], w.eps[:], ACT.Gelu).then_inc(a_own, own.one())
            act.wait_ge(a_own, own.n)
            for step, g, q in turns(act, TF + 1, NG, own, late=(Z5, H1, GATE)):
                if step == T1:
                    act.wait_ge(t1_ready, g + 1)
                    nc.scalar.activation(xt[:], p_t[0:D + 3, :], ACT.Identity).then_inc(xt_ready, 1)
                if step == Z1:
                    act.wait_ge(bias[1], g + 1)
                    normalise(1, lambda j: p_tm[:, j, :], rs[1], nb[1])
                if step == E2:
                    act.wait_ge(bias[2], g + 1)
                    normalise(2, lambda j: h0[:, j, :], rs[2], nb[2])
                    nc.scalar.activation(seqs(g), h0[:], ACT.Identity).then_inc(a_own, own.one())
                if step == Z3:
                    act.wait_ge(bias[3], g + 1)
                    normalise(3, lambda j: p_gr[:, j * D:(j + 1) * D], rs[3], nb[3])
                if step == H1:
                    act.wait_ge(bias[4], g + 1)
                    normalise(4, lambda j: p_tm[:, j, :], rs[4], nb[4])
                if step == Z5:
                    act.wait_ge(bias[5], g + 1)
                    normalise(5, lambda j: h1[:, j, :], rr5, nb[5])
                if step in (T2, T3, T4):
                    k, dst = {T2: (2, et_in), T3: (3, at_in), T4: (5, xs[q])}[step]
                    act.wait_ge(t_ready[k], g + 1)
                    nc.scalar.activation(dst[:], p_t[:], ACT.Identity).then_inc(in_ready[k], 1)
                if step == U:
                    act.wait_ge(u_psum, g + 1)
                    nc.scalar.activation(u[:], p_u[:], ACT.Relu).then_inc(u_ready, 1)
                if step == R:
                    act.wait_ge(r_psum, g + 1)
                    nc.scalar.activation(ab[:], p_gr[:], ACT.Copy, scale=DECAY).then_inc(ab_ready, 1)
                if step == GATE:
                    act.wait_ge(gap_ready, g + 1)
                    nc.scalar.activation(th[:], gap[:], ACT.Tanh, scale=0.5).then_inc(th_ready, 1)
                if step == WT:
                    act.wait_ge(gt_psum, g + 1)
                    if some(g * 16):
                        act.wait_ge(gt_stored, g * 16)
                    nc.scalar.activation(gt[:], p_u[0:G * NE, 1, 0:P], ACT.Identity).then_inc(a_own, own.one())
                    if some((g - 1) * NPAIR):
                        act.wait_ge(part_ready, (g - 1) * NPAIR)
                    act.wait_ge(a_own, own.n)
                    act.dma_start(w.gates[0][:, bass.ds(g * GT, GT)].rearrange("e (j t) -> j e t", j=G),
                                  gt[:]).then_inc(gt_stored, 16)
                if step in (F0, F1, F2, F3):
                    p = (F0, F1, F2, F3, F4).index(step)
                    for half in range(2):
                        e = 2 * p + half
                        act.wait_ge(up_psum, g * NE + (e + 1))
                        nc.scalar.activation(hid[:, p % 2, half, :], p_h[:, half, :], ACT.Gelu,
                                             bias=w.f0_b1[:, e, 0:1]).then_inc(hid_ready, 1)

        @block.vector
        def _(dve):
            own = Order(dve, d_own)

            def moments(k, src):
                for j in range(G):
                    last = nc.vector.bn_stats(bn[k][:, j, :], src(j))
                last.then_inc(d_own, own.one())
                dve.wait_ge(d_own, own.n)
                for j in range(G):
                    last = nc.vector.bn_aggr(st[k][:, j, :], bn[k][:, j, :])
                last.then_inc(stats[k], 1)

            def offset(k, scale):
                nc.vector.scalar_tensor_tensor(nb[k][:], st[k][:, :, 0], -1.0, scale[:], ALU.mult,
                                               ALU.mult).then_inc(bias[k], 1)

            def normal_variance(k):
                nc.vector.tensor_tensor(vn[k][:], rs[k][:], rs[k][:], ALU.mult).then_inc(d_own, own.one())
                dve.wait_ge(d_own, own.n)
                nc.vector.tensor_tensor(vn[k][:], vn[k][:], st[k][:, :, 1], ALU.mult).then_inc(vn_ready[k], 1)

            def parts(k):
                nc.vector.tensor_copy(split[k][:, :, 0:D], z[k][:]).then_inc(d_own, own.one())
                dve.wait_ge(d_own, own.n)
                nc.vector.tensor_tensor(split[k][:, :, D:2 * D], z[k][:], split[k][:, :, 0:D].bitcast(F32),
                                        ALU.subtract).then_inc(split_ready[k], 1)

            nc.vector.memset(sig[:, 0:1], 0.0).then_inc(d_own, own.one())
            dve.wait_ge(d_own, own.n)
            for step, g, q in turns(dve, TF + 1, NG, own, late=(S, R, H1, GATE)):
                if step == PROJ:
                    dve.wait_ge(proj_ready, g + 1)
                    moments(1, lambda j: p_tm[:, j, :])
                if step == STATS2:
                    dve.wait_ge(h0_ready, g + 1)
                    moments(2, lambda j: h0[:, j, :])
                if step == A:
                    dve.wait_ge(a_ready, g + 1)
                    moments(3, lambda j: p_gr[:, j * D:(j + 1) * D])
                if step == V:
                    dve.wait_ge(v_ready, g + 1)
                    moments(4, lambda j: p_tm[:, j, :])
                if step == STATS5:
                    dve.wait_ge(h1_ready, g + 1)
                    moments(5, lambda j: h1[:, j, :])
                if step in (Z1, E2, Z3, H1):
                    k = {Z1: 1, E2: 2, Z3: 3, H1: 4}[step]
                    dve.wait_ge(rstd[k], g + 1)
                    offset(k, rs[k])
                if step == E2:
                    normal_variance(2)
                if step == V5:
                    dve.wait_ge(rstd[5], g + 1)
                    normal_variance(5)
                if step == Z5:
                    dve.wait_ge(rn_ready[5], g + 1)
                    nc.vector.tensor_tensor(rr5[:], rs[5][:], rn[5][:], ALU.mult).then_inc(d_own, own.one())
                    dve.wait_ge(d_own, own.n)
                    offset(5, rr5)
                if step in (D2, D3, D5):
                    k = {D2: 2, D3: 3, D5: 5}[step]
                    dve.wait_ge(z_ready[k], g + 1)
                    parts(k)
                if step == S:
                    dve.wait_ge(s_ready, g + 1)
                    nc.vector.tensor_copy(s_c[:], p_u[0:G, 0, 0:P]).then_inc(d_own, own.one())
                    dve.wait_ge(d_own, own.n)
                    nc.vector.tensor_tensor_scan(m_c[:], s_c[:], s_c[:], 0.0, ALU.max, ALU.max).then_inc(d_own, own.one())
                    for _ in range(4):
                        dve.wait_ge(d_own, own.n)
                        nc.vector.tensor_scalar(sig[:, 1:P + 1], m_c[:], DECAY / TINY, None, ALU.mult).then_inc(d_own, own.one())
                        dve.wait_ge(d_own, own.n)
                        nc.vector.scalar_tensor_tensor(m_c[:], sig[:, 0:P], DECAY, s_c[:], ALU.min, ALU.add).then_inc(d_own, own.one())
                    dve.wait_ge(d_own, own.n)
                    nc.vector.tensor_scalar(m_c[:], m_c[:], TINY, None, ALU.max).then_inc(d_own, own.one())
                    dve.wait_ge(d_own, own.n)
                    nc.vector.reciprocal(r_c[:], m_c[:]).then_inc(r_ready, 1)
                if step == R:
                    dve.wait_ge(ab_ready, g + 1)
                    nc.vector.tensor_tensor(d_in[:], u[:], rows(p_gr[:], NCH), ALU.mult).then_inc(d_own, own.one())
                    dve.wait_ge(d_own, own.n)
                    for c in range(NCH):
                        for j in range(G):
                            tile = slice(j * P, (j + 1) * P)
                            last = nc.vector.tensor_tensor_scan(x[q][:, c, tile], ab[:, tile], d_in[:, c, tile], 0.0,
                                                                ALU.mult, ALU.add)
                    last.then_inc(x_ready, 1)
                if step == GRAM:
                    dve.wait_ge(gram_ready, g + 1)
                    nc.vector.tensor_tensor(pm[:].rearrange("p (j t) -> p j t", j=G),
                                            p_gr[:].rearrange("p (j t) -> p j t", j=G),
                                            rows(w.decay[:], G), ALU.mult).then_inc(pm_ready, 1)
                if step == Y:
                    dve.wait_ge(y_psum, g + 1)
                    nc.vector.scalar_tensor_tensor(y[:], p_u[:], 0.0, x[q][:], ALU.max, ALU.mult).then_inc(y_ready, 1)
                if step == H1:
                    dve.wait_ge(z_ready[4], g + 1)
                    nc.vector.tensor_tensor(h1[:], seqs(g), z[4][:], ALU.add).then_inc(h1_ready, 1)
                    nc.vector.tensor_tensor(seqs(g), seqs(g), z[4][:], ALU.add).then_inc(d_own, own.one())
                if step == GATE:
                    dve.wait_ge(logit_psum, g + 1)
                    nc.vector.tensor_tensor(logits[:], p_tm[:, 0, 0:G * NE].rearrange("p (j e) -> p j e", j=G),
                                            rows(w.f0_br[:], G), ALU.add).then_inc(d_own, own.one())
                    dve.wait_ge(d_own, own.n)
                    for j in range(G):
                        last = nc.vector.max(top[:, j, :], logits[:, j, :])
                    last.then_inc(d_own, own.one())
                    dve.wait_ge(d_own, own.n)
                    nc.vector.tensor_tensor(gap[:], top[:, :, 0], top[:, :, 1], ALU.subtract).then_inc(gap_ready, 1)
                if step == W:
                    for j in range(G):
                        last = nc.vector.max_index(ix[:, j, :], top[:, j, :], logits[:, j, :])
                    last.then_inc(d_own, own.one())
                    dve.wait_ge(d_own, own.n)
                    nc.vector.tensor_copy(ixf[:], ix[:, :, 0:2]).then_inc(d_own, own.one())
                    dve.wait_ge(d_own, own.n)
                    for k in range(2):
                        nc.vector.tensor_tensor(eq[:, k, :, :], rows(w.iota_e[:], G), wide(ixf[:, :, k], NE),
                                                ALU.is_equal).then_inc(d_own, own.one())
                    dve.wait_ge(th_ready, g + 1)
                    nc.vector.tensor_scalar(wt2[:, :, 0], th[:], 0.5, 0.5, ALU.mult, ALU.add).then_inc(d_own, own.one())
                    nc.vector.tensor_scalar(wt2[:, :, 1], th[:], -0.5, 0.5, ALU.mult, ALU.add).then_inc(d_own, own.one())
                    dve.wait_ge(d_own, own.n)
                    for k in range(2):
                        nc.vector.tensor_tensor(eq[:, k, :, :], eq[:, k, :, :], wide(wt2[:, :, k], NE),
                                                ALU.mult).then_inc(d_own, own.one())
                    dve.wait_ge(d_own, own.n)
                    nc.vector.tensor_tensor(gate[:], eq[:, 0, :, :], eq[:, 1, :, :], ALU.add).then_inc(gate_ready, 1)
                if step in (F1, F2, F3, F4):
                    p = (F1, F2, F3, F4).index(step)
                    dve.wait_ge(down_psum, g * NPAIR + (p + 1))
                    if p == 0:
                        dve.wait_ge(wb_loaded[q], parity_count(g, q, 32))
                        if some(g - 1):
                            dve.wait_ge(tf_ready, g - 1)
                    elif p == 1:
                        if some(g * (NPAIR - 1)):
                            dve.wait_ge(acc_ready, g * (NPAIR - 1))
                    elif p == NPAIR - 1:
                        if some(g * (NPAIR - 1) + (p - 2)):
                            dve.wait_ge(acc_ready, g * (NPAIR - 1) + (p - 2))
                    dst = part[:, p % 2, :] if p else acc[q][:]
                    nc.vector.scalar_tensor_tensor(dst, p_y[:], w.f0_b2[:, p:p + 1], wb[q][:, p, :], ALU.add,
                                                   ALU.mult).then_inc(part_ready, 1)
                if step == TF:
                    dve.wait_ge(tf_ready, g + 1)
                    halves = p_t[:].rearrange("p (j two d) -> p two j d", j=G, two=2)
                    nc.vector.tensor_tensor(seqs(g), seqs(g), halves[:, 0], ALU.add).then_inc(d_own, own.one())
                    dve.wait_ge(d_own, own.n)
                    nc.vector.tensor_tensor(seqs(g), seqs(g), halves[:, 1], ALU.add).then_inc(h2_ready, 1)

        @block.sync
        def _(sp):
            own = Order(sp, s_own)
            for step, g, q in turns(sp, TF + 1, NG, own):
                if step == WT:
                    cols = bass.ds(held(sp, g * GT), GT)
                    sp.wait_ge(gt_stored, g * 16 + 16)
                    for half in range(2):
                        src = w.gates[0].rearrange("(p two) t -> two p t", two=2)[half][:, cols]
                        sp.dma_start(wb[q][half * D:half * D + D, :, :],
                                     src.unsqueeze(0).to_broadcast([D, NPAIR, GT])).then_inc(wb_loaded[q], 16)
            if out is not None:
                sp.wait_ge(h2_ready, NG)
                sp.dma_start(out.rearrange("b t d -> t b d"), w.h_all[:]).then_inc(stored, 16)
                sp.wait_ge(stored, 16)


(L_STATS, L_Z, L_D, L_T, L_QKV, L_SCORE, L_EXP, _L7,
 L_PT, L_OUT, M_STATS, M_Z, M_D, M_T, M_GATE, M_W,
 M_WT, _M17, _M18, _M19, M_F0, _M21, _M22, _M23,
 _M24, _M25, _M26, _M27, _M28, M_FLAST, M_SUM, _M31,
 _M32, _M33, M_TF) = range(35)


def _layer1(nc, a, w, NG, stage, out):
    def sb(name, shape, dt=F32):
        return stage.enter_context(nc.sbuf_tensor("l1_" + name, shape, dt))

    def ps(name, shape):
        return stage.enter_context(nc.psum_tensor("l1_" + name, shape, F32))

    def sem(name):
        return stage.enter_context(nc.semaphore("l1_" + name))

    st = {k: sb(f"st{k}", [P, G, 2]) for k in range(2)}
    bn = {k: sb(f"bn{k}", [P, G, 6]) for k in range(2)}
    ve = {k: sb(f"ve{k}", [P, G]) for k in range(2)}
    rs = {k: sb(f"rs{k}", [P, G]) for k in range(2)}
    z = {k: sb(f"z{k}", [P, G, D]) for k in range(2)}
    h3 = sb("h3", [P, G, D])
    split = {k: sb(f"split{k}", [P, G, 2 * D], F32R) for k in range(2)}
    xa = sb("xa", [P, GT], F32R)
    xs = [sb(f"xs{q}", [P, GT], F32R) for q in range(2)]
    qt, kt = sb("qt", [D, GT]), sb("kt", [D, GT])
    vp = sb("vp", [P, G, D + 2])
    top_s, nmax, total = sb("top_s", [P, G]), sb("nmax", [P, G]), sb("total", [P, G])
    prob, pt = sb("prob", [P, GT]), sb("pt", [P, GT])
    live, coef = sb("live", [P, G, 2]), sb("coef", [P, G])
    inv = sb("inv", [P, G])
    o = sb("o", [P, G, D])
    logits, top = sb("logits", [P, G, NE]), sb("top", [P, G, NE])
    ix, ixf = sb("ix", [P, G, NE], U32), sb("ixf", [P, G, 2])
    gap, th, wt2 = sb("gap", [P, G]), sb("th", [P, G]), sb("wt2", [P, G, 2])
    eq = sb("eq", [P, 2, G, NE])
    gate = sb("gate", [P, G, NE])
    gt = sb("gt", [G * NE, P])
    wb = [sb(f"wb{q}", [P, NE // 2, GT]) for q in range(2)]
    hid = sb("hid", [P, 4, 2, GT])
    part = sb("part", [P, 2, GT])
    acc = [sb(f"acc{q}", [P, GT]) for q in range(2)]

    p_t, p_sc, p_gr = ps("p_t", [P, 512]), ps("p_sc", [P, 512]), ps("p_gr", [P, 512])
    p_h, p_y = ps("p_h", [P, 2, 2, GT]), ps("p_y", [P, GT])

    stats = {k: sem(f"stats{k}") for k in range(2)}
    rstd = {k: sem(f"rstd{k}") for k in range(2)}
    z_ready = {k: sem(f"z_ready{k}") for k in range(2)}
    split_ready = {k: sem(f"split_ready{k}") for k in range(2)}
    t_ready = {k: sem(f"t_ready{k}") for k in range(2)}
    in_ready = {k: sem(f"in_ready{k}") for k in range(2)}
    qk_psum, v_psum, q_ready, k_ready, v_ready = (sem(n) for n in ("qk_psum", "v_psum", "q_ready", "k_ready", "v_ready"))
    score_psum, top_ready, prob_ready, pt_psum, pt_ready = (
        sem(n) for n in ("score_psum", "top_ready", "prob_ready", "pt_psum", "pt_ready"))
    hb_ready, o_psum, h3_ready = sem("hb_ready"), sem("o_psum"), sem("h3_ready")
    logit_psum, gap_ready, th_ready = sem("logit_psum"), sem("gap_ready"), sem("th_ready")
    gate_ready, gt_psum, gt_stored = sem("gate_ready"), sem("gt_psum"), sem("gt_stored")
    wb_loaded = [sem(f"wb_loaded{q}") for q in range(2)]
    up_psum, hid_ready, down_psum = sem("up_psum"), sem("hid_ready"), sem("down_psum")
    part_ready, acc_ready, tf_ready, h4_ready = sem("part_ready"), sem("acc_ready"), sem("tf_ready"), sem("h4_ready")
    d_own, a_own, p_own, t_own, s_own = sem("d_own"), sem("a_own"), sem("p_own"), sem("t_own"), sem("s_own")
    stored = sem("stored")

    NPAIR = NE // 2
    CH = w.f1_w2.shape[2]
    NST = NPAIR * CH
    assert M_FLAST == M_F0 + NST + 1
    H1 = CH * P

    def seqs(g):
        return w.h_all[:, bass.ds(g * G, G), :]

    def ahead(g, n):
        return min(g + n, NG) if isinstance(g, int) else g + n

    with nc.Block() as block:
        @block.gpsimd
        def _(pool):
            own = Order(pool, p_own)
            for step, g, q in turns(pool, M_TF + 1, NG, own):
                if step in (L_STATS, M_STATS):
                    k = (L_STATS, M_STATS).index(step)
                    pool.wait_ge(stats[k], g + 1)
                    nc.gpsimd.tensor_tensor(ve[k][:], st[k][:, :, 1], w.eps[:], ALU.add).then_inc(p_own, own.one())
                    pool.wait_ge(p_own, own.n)
                    nc.gpsimd.tensor_tensor(rs[k][:], ve[k][:], w.mhalf[:], ALU.pow).then_inc(rstd[k], 1)
                if step == L_T:
                    pool.wait_ge(z_ready[0], g + 1)
                    nc.gpsimd.tensor_tensor(seqs(g), seqs(g), rows(w.bo[:], G), ALU.add).then_inc(hb_ready, 1)
                if M_F0 < step <= M_SUM and (step - M_F0 - 2) % CH == 0:
                    p = (step - M_F0 - 2) // CH - 1
                    if p > 0:
                        pool.wait_ge(part_ready, g * NPAIR + (p + 1))
                        nc.gpsimd.tensor_tensor(acc[q][:], acc[q][:], part[:, p % 2, :], ALU.add).then_inc(acc_ready, 1)
                        if p < NPAIR - 1:
                            if some(g * (NPAIR - 1) + p):
                                pool.wait_ge(acc_ready, g * (NPAIR - 1) + p)

        @block.tensor
        def _(pe):
            own = Order(pe, t_own)

            def transposes(src):
                for j in range(G):
                    last = nc.tensor.transpose(p_t[:, j * P:(j + 1) * P], src(j), w.ident[:])
                return last

            def stacked(dst, hi, lo, moving):
                nc.tensor.matmul(dst, hi, moving, start=True, stop=False)
                return nc.tensor.matmul(dst, lo, moving, start=False, stop=True)

            for step, g, q in turns(pe, M_TF + 1, NG, own, late=(L_OUT,)):
                if step in (L_T, M_T):
                    k = (L_T, M_T).index(step)
                    pe.wait_ge(split_ready[k], g + 1)
                    if k:
                        pe.wait_ge(in_ready[0], ahead(g, 2))
                    transposes(lambda j: split[k][:, j, :].bitcast(F32)).then_inc(t_ready[k], 1)
                if step == L_QKV:
                    pe.wait_ge(in_ready[0], g + 1)
                    stacked(p_sc[:], w.wqk_hi[:], w.wqk_lo[:], xa[:]).then_inc(qk_psum, 1)
                    for j in range(G):
                        last = nc.tensor.matmul(p_gr[:, j * (D + 2):(j + 1) * (D + 2)],
                                                xa[:, j * P:(j + 1) * P].bitcast(F32), w.wv2[:], start=True, stop=True)
                    last.then_inc(v_psum, 1)
                if step == L_SCORE:
                    pe.wait_ge(q_ready, g + 1)
                    pe.wait_ge(k_ready, g + 1)
                    for j in range(G):
                        tile = slice(j * P, (j + 1) * P)
                        last = nc.tensor.matmul(p_sc[:, tile], qt[:, tile], kt[:, tile], start=True, stop=True)
                    last.then_inc(score_psum, 1)
                if step == L_PT:
                    pe.wait_ge(prob_ready, g + 1)
                    transposes(lambda j: prob[:, j * P:(j + 1) * P]).then_inc(pt_psum, 1)
                if step == L_OUT:
                    pe.wait_ge(pt_ready, g + 1)
                    pe.wait_ge(v_ready, g + 1)
                    for j in range(G):
                        last = nc.tensor.matmul(p_gr[:, j * D:(j + 1) * D], pt[:, j * P:(j + 1) * P], vp[:, j, 0:D],
                                                start=True, stop=True)
                    last.then_inc(o_psum, 1)
                if step == M_GATE:
                    pe.wait_ge(in_ready[1], g + 1)
                    pe.wait_ge(v_ready, ahead(g, 2))
                    for j in range(G):
                        last = nc.tensor.matmul(p_gr[:, j * NE:(j + 1) * NE],
                                                xs[q][:, j * P:(j + 1) * P].bitcast(F32), w.f1_wr[:],
                                                start=True, stop=True)
                    last.then_inc(logit_psum, 1)
                if step == M_WT:
                    pe.wait_ge(gate_ready, g + 1)
                    nc.tensor.transpose(p_gr[0:G * NE, 0:P], gate[:].rearrange("p g e -> p (g e)"),
                                        w.ident[:]).then_inc(gt_psum, 1)
                if M_F0 <= step <= M_FLAST:
                    s = step - M_F0
                    if s >= 2:
                        p, c = divmod(s - 2, CH)
                        pe.wait_ge(hid_ready, g * NST + (s - 1))
                        if c == 0:
                            if some(g * NPAIR + p):
                                pe.wait_ge(part_ready, g * NPAIR + p)
                        for half in range(2):
                            last = nc.tensor.matmul(p_y[half * D:half * D + D, :], w.f1_w2[:, 2 * p + half, c, :],
                                                    hid[:, (s - 2) % 4, half, :], start=(c == 0), stop=(c == CH - 1))
                        if c == CH - 1:
                            last.then_inc(down_psum, 1)
                    if s < NST:
                        p, c = divmod(s, CH)
                        for half in range(2):
                            at = (2 * p + half) * H1 + c * P
                            last = stacked(p_h[:, s % 2, half, :], w.f1_w1_hi[:, at:at + P], w.f1_w1_lo[:, at:at + P],
                                           xs[q][:])
                            last.then_inc(up_psum, 1)
                if step == M_TF:
                    pe.wait_ge(acc_ready, g * (NPAIR - 1) + (NPAIR - 1))
                    pe.wait_ge(pt_ready, ahead(g, M_TF // K))
                    transposes(lambda j: acc[q][:, j * P:(j + 1) * P]).then_inc(tf_ready, 1)

        @block.scalar
        def _(act):
            own = Order(act, a_own)
            for step, g, q in turns(act, M_TF + 1, NG, own, late=(M_GATE,)):
                if step in (L_T, M_T):
                    k, dst = ((0, xa), (1, xs[q]))[step == M_T]
                    act.wait_ge(t_ready[k], g + 1)
                    nc.scalar.activation(dst[:], p_t[:], ACT.Identity).then_inc(in_ready[k], 1)
                if step == L_QKV:
                    act.wait_ge(qk_psum, g + 1)
                    nc.scalar.activation(qt[:], p_sc[0:D, :], ACT.Identity, bias=w.bqk[0:D, :]).then_inc(q_ready, 1)
                if step == L_EXP:
                    act.wait_ge(top_ready, g + 1)
                    for j in range(G):
                        tile = slice(j * P, (j + 1) * P)
                        last = nc.scalar.activation(prob[:, tile], p_sc[:, tile], ACT.Exp, bias=nmax[:, j:j + 1],
                                                    scale=float(D) ** -0.5, accum_out=total[:, j:j + 1])
                    last.then_inc(prob_ready, 1)
                if step == L_PT:
                    act.wait_ge(pt_psum, g + 1)
                    nc.scalar.activation(pt[:], p_t[:], ACT.Identity).then_inc(pt_ready, 1)
                if step == M_GATE:
                    act.wait_ge(gap_ready, g + 1)
                    nc.scalar.activation(th[:], gap[:], ACT.Tanh, scale=0.5).then_inc(th_ready, 1)
                if step == M_WT:
                    act.wait_ge(gt_psum, g + 1)
                    if some(g * 16):
                        act.wait_ge(gt_stored, g * 16)
                    nc.scalar.activation(gt[:], p_gr[0:G * NE, 0:P], ACT.Identity).then_inc(a_own, own.one())
                    if some((g - 1) * NPAIR):
                        act.wait_ge(part_ready, (g - 1) * NPAIR)
                    act.wait_ge(a_own, own.n)
                    act.dma_start(w.gates[1][:, bass.ds(g * GT, GT)].rearrange("e (j t) -> j e t", j=G),
                                  gt[:]).then_inc(gt_stored, 16)
                if M_F0 <= step < M_F0 + NST:
                    s = step - M_F0
                    p, c = divmod(s, CH)
                    for half in range(2):
                        act.wait_ge(up_psum, g * (2 * NST) + (2 * s + half + 1))
                        last = nc.scalar.activation(hid[:, s % 4, half, :], p_h[:, s % 2, half, :], ACT.Gelu,
                                                    bias=w.f1_b1[:, 2 * p + half, c:c + 1])
                        if half:
                            last.then_inc(hid_ready, 1)

        @block.vector
        def _(dve):
            own = Order(dve, d_own)

            for step, g, q in turns(dve, M_TF + 1, NG, own, late=(L_OUT,)):
                if step in (L_STATS, M_STATS):
                    k = (L_STATS, M_STATS).index(step)
                    if k:
                        dve.wait_ge(h3_ready, g + 1)
                    for j in range(G):
                        src = h3[:, j, :] if k else w.h_all[:, bass.ds(g * G + j, 1), :]
                        last = nc.vector.bn_stats(bn[k][:, j, :], src)
                    last.then_inc(d_own, own.one())
                    dve.wait_ge(d_own, own.n)
                    for j in range(G):
                        last = nc.vector.bn_aggr(st[k][:, j, :], bn[k][:, j, :])
                    last.then_inc(stats[k], 1)
                if step in (L_Z, M_Z):
                    k = (L_Z, M_Z).index(step)
                    dve.wait_ge(rstd[k], g + 1)
                    for j in range(G):
                        src = h3[:, j, :] if k else w.h_all[:, bass.ds(g * G + j, 1), :]
                        dst = z[k][:, j, :] if k else z[k][:, j:j + 1, :]
                        last = nc.vector.tensor_scalar(dst, src, st[k][:, j, 0:1], rs[k][:, j:j + 1],
                                                       ALU.subtract, ALU.mult)
                    last.then_inc(z_ready[k], 1)
                if step in (L_D, M_D):
                    k = (L_D, M_D).index(step)
                    dve.wait_ge(z_ready[k], g + 1)
                    nc.vector.tensor_copy(split[k][:, :, 0:D], z[k][:]).then_inc(d_own, own.one())
                    dve.wait_ge(d_own, own.n)
                    nc.vector.tensor_tensor(split[k][:, :, D:2 * D], z[k][:], split[k][:, :, 0:D].bitcast(F32),
                                            ALU.subtract).then_inc(split_ready[k], 1)
                if step == L_QKV:
                    dve.wait_ge(qk_psum, g + 1)
                    nc.vector.tensor_scalar(kt[:], p_sc[D:P, :], w.bqk[D:P, :], None, ALU.add).then_inc(k_ready, 1)
                    dve.wait_ge(v_psum, g + 1)
                    nc.vector.tensor_tensor(vp[:], p_gr[:, 0:G * (D + 2)].rearrange("p (j d) -> p j d", j=G),
                                            rows(w.bv2[:], G), ALU.add).then_inc(v_ready, 1)
                if step == L_SCORE:
                    dve.wait_ge(score_psum, g + 1)
                    nc.vector.reduce_max(top_s[:], p_sc[:].rearrange("p (j t) -> p j t", j=G), AX.X).then_inc(d_own, own.one())
                    dve.wait_ge(d_own, own.n)
                    nc.vector.tensor_scalar(nmax[:], top_s[:], -float(D) ** -0.5, None, ALU.mult).then_inc(top_ready, 1)
                if step == L_PT:
                    dve.wait_ge(prob_ready, g + 1)
                    nc.vector.reciprocal(inv[:], total[:]).then_inc(d_own, own.one())
                    dve.wait_ge(v_ready, g + 1)
                    nc.vector.tensor_scalar(live[:], vp[:, :, D:D + 2], 0.0, None, ALU.not_equal).then_inc(d_own, own.one())
                    dve.wait_ge(d_own, own.n)
                    nc.vector.tensor_tensor(coef[:], live[:, :, 0], live[:, :, 1], ALU.mult).then_inc(d_own, own.one())
                    dve.wait_ge(d_own, own.n)
                    nc.vector.tensor_tensor(coef[:], coef[:], inv[:], ALU.mult).then_inc(d_own, own.one())
                    dve.wait_ge(d_own, own.n)
                if step == L_OUT:
                    dve.wait_ge(o_psum, g + 1)
                    nc.vector.tensor_tensor(o[:], p_gr[:, 0:G * D].rearrange("p (j d) -> p j d", j=G),
                                            wide(coef[:], D), ALU.mult).then_inc(d_own, own.one())
                    dve.wait_ge(d_own, own.n)
                    dve.wait_ge(hb_ready, g + 1)
                    nc.vector.tensor_tensor(h3[:], seqs(g), o[:], ALU.add).then_inc(h3_ready, 1)
                    nc.vector.tensor_tensor(seqs(g), seqs(g), o[:], ALU.add).then_inc(d_own, own.one())
                if step == M_GATE:
                    dve.wait_ge(logit_psum, g + 1)
                    nc.vector.tensor_tensor(logits[:], p_gr[:, 0:G * NE].rearrange("p (j e) -> p j e", j=G),
                                            rows(w.f1_br[:], G), ALU.add).then_inc(d_own, own.one())
                    dve.wait_ge(d_own, own.n)
                    for j in range(G):
                        last = nc.vector.max(top[:, j, :], logits[:, j, :])
                    last.then_inc(d_own, own.one())
                    dve.wait_ge(d_own, own.n)
                    nc.vector.tensor_tensor(gap[:], top[:, :, 0], top[:, :, 1], ALU.subtract).then_inc(gap_ready, 1)
                if step == M_W:
                    for j in range(G):
                        last = nc.vector.max_index(ix[:, j, :], top[:, j, :], logits[:, j, :])
                    last.then_inc(d_own, own.one())
                    dve.wait_ge(d_own, own.n)
                    nc.vector.tensor_copy(ixf[:], ix[:, :, 0:2]).then_inc(d_own, own.one())
                    dve.wait_ge(d_own, own.n)
                    for k in range(2):
                        nc.vector.tensor_tensor(eq[:, k, :, :], rows(w.iota_e[:], G), wide(ixf[:, :, k], NE),
                                                ALU.is_equal).then_inc(d_own, own.one())
                    dve.wait_ge(th_ready, g + 1)
                    nc.vector.tensor_scalar(wt2[:, :, 0], th[:], 0.5, 0.5, ALU.mult, ALU.add).then_inc(d_own, own.one())
                    nc.vector.tensor_scalar(wt2[:, :, 1], th[:], -0.5, 0.5, ALU.mult, ALU.add).then_inc(d_own, own.one())
                    dve.wait_ge(d_own, own.n)
                    for k in range(2):
                        nc.vector.tensor_tensor(eq[:, k, :, :], eq[:, k, :, :], wide(wt2[:, :, k], NE),
                                                ALU.mult).then_inc(d_own, own.one())
                    dve.wait_ge(d_own, own.n)
                    nc.vector.tensor_tensor(gate[:], eq[:, 0, :, :], eq[:, 1, :, :], ALU.add).then_inc(gate_ready, 1)
                if M_F0 + CH < step <= M_FLAST and (step - M_F0 - 1) % CH == 0:
                    p = (step - M_F0 - 1) // CH - 1
                    dve.wait_ge(down_psum, g * NPAIR + (p + 1))
                    if p == 0:
                        dve.wait_ge(wb_loaded[q], parity_count(g, q, 32))
                        if some(g - 1):
                            dve.wait_ge(tf_ready, g - 1)
                    elif p == 1:
                        if some(g * (NPAIR - 1)):
                            dve.wait_ge(acc_ready, g * (NPAIR - 1))
                    elif p == NPAIR - 1:
                        if some(g * (NPAIR - 1) + (p - 2)):
                            dve.wait_ge(acc_ready, g * (NPAIR - 1) + (p - 2))
                    dst = part[:, p % 2, :] if p else acc[q][:]
                    nc.vector.scalar_tensor_tensor(dst, p_y[:], w.f1_b2[:, p:p + 1], wb[q][:, p, :], ALU.add,
                                                   ALU.mult).then_inc(part_ready, 1)
                if step == M_TF:
                    dve.wait_ge(tf_ready, g + 1)
                    halves = p_t[:].rearrange("p (j two d) -> p two j d", j=G, two=2)
                    nc.vector.tensor_tensor(seqs(g), seqs(g), halves[:, 0], ALU.add).then_inc(d_own, own.one())
                    dve.wait_ge(d_own, own.n)
                    nc.vector.tensor_tensor(seqs(g), seqs(g), halves[:, 1], ALU.add).then_inc(h4_ready, 1)

        @block.sync
        def _(sp):
            own = Order(sp, s_own)
            for step, g, q in turns(sp, M_TF + 1, NG, own):
                if step == M_WT:
                    cols = bass.ds(held(sp, g * GT), GT)
                    sp.wait_ge(gt_stored, g * 16 + 16)
                    for half in range(2):
                        src = w.gates[1].rearrange("(p two) t -> two p t", two=2)[half][:, cols]
                        sp.dma_start(wb[q][half * D:half * D + D, :, :],
                                     src.unsqueeze(0).to_broadcast([D, NPAIR, GT])).then_inc(wb_loaded[q], 16)
                if step == M_TF:
                    sp.wait_ge(h4_ready, g + 1)
                    sp.dma_start(out[bass.ds(g * G, G), :, :].rearrange("b t d -> t b d"), seqs(g)).then_inc(stored, 16)
            sp.wait_ge(stored, 16 * NG)


def kernel(**inputs):
    import numpy as _np
    import concourse.bacc as _bacc
    from concourse import mybir as _mybir
    from concourse.bass_utils import run_bass_kernel_spmd as _run

    nc = _bacc.Bacc("TRN2", target_bir_lowering=False, num_devices=1)
    arrays, aps = {}, {}
    for name, value in inputs.items():
        value = _np.ascontiguousarray(value)
        arrays[f"in_{name}"] = value
        aps[name] = nc.dram_tensor(f"in_{name}", value.shape, _mybir.dt.from_np(value.dtype), kind="ExternalInput").ap()
    shape = (*inputs["x"].shape, inputs["L0_tok_h_q"].shape[1])
    out = nc.dram_tensor("out", shape, _mybir.dt.float32, kind="ExternalOutput").ap()
    tower(nc, aps, out)
    return _run(nc, [arrays], core_ids=[0]).results[0]["out"]
```
